# Optimizing a Trainium2 kernel written in Bass

```python
import numpy as np
import jax
import jax.numpy as jnp

def _softmax(x, axis=-1):
    return jax.nn.softmax(x, axis=axis)

def _gelu(x):
    return jax.nn.gelu(x, approximate=True)

def _silu(x):
    return jax.nn.silu(x)

def _sigmoid(x):
    return jax.nn.sigmoid(x)

def _layernorm(x, axis=-1, eps=1e-05):
    m = jnp.mean(x, axis=axis, keepdims=True)
    v = jnp.var(x, axis=axis, keepdims=True)
    return (x - m) / jnp.sqrt(v + eps)

def _scatter_add(tgt, idx, src, axis=0):
    return tgt.at[idx].add(src)

def _segment_sum(src, seg, n):
    return jax.ops.segment_sum(src, seg, n)
kernel_name = 'mk_prb_d1_jaxref_r4_e408e8'

def setup_inputs(seed: int=0):
    np.random.seed(seed)
    _w = jnp.asarray

    def _L0_attn_setup():
        import jax, jax.numpy as jnp
        import numpy as np
        EPS = 0.0001
        key = jax.random.key(seed)
        ks = jax.random.split(key, 8)
        B, S, D, N = (4, 1024, 256, 64)
        return {'tokens': jax.random.normal(ks[0], (B, S, D), dtype=jnp.float32), 'norm_w': jnp.ones((D,), dtype=jnp.float32), 'W_in': jax.random.normal(ks[1], (N, D), dtype=jnp.float32) * (1.0 / np.sqrt(D)), 'b_in': jax.random.normal(ks[2], (N,), dtype=jnp.float32) * 0.02, 'W_out': jax.random.normal(ks[3], (D, N), dtype=jnp.float32) * (1.0 / np.sqrt(N)), 'b_out': jax.random.normal(ks[4], (D,), dtype=jnp.float32) * 0.02, 'W_skip': jax.random.normal(ks[5], (D, D), dtype=jnp.float32) * (1.0 / np.sqrt(D)), 'b_skip': jax.random.normal(ks[6], (D,), dtype=jnp.float32) * 0.02, 'log_decay': jnp.zeros((N,), dtype=jnp.float32)}
    _L0_attn_in = _L0_attn_setup()

    def _L0_ffn_setup():
        import jax, jax.numpy as jnp
        import numpy as np
        B, S, H, I, E = (2, 1024, 256, 128, 8)
        key = jax.random.key(seed)
        ks = jax.random.split(key, 5)
        scale_h = 1.0 / np.sqrt(H)
        scale_i = 1.0 / np.sqrt(I)
        return {'hidden_states': jax.random.normal(ks[0], (B, S, H), dtype=jnp.float32), 'gate_w': jax.random.normal(ks[1], (E, H), dtype=jnp.float32) * scale_h, 'w_gate': jax.random.normal(ks[2], (E, I, H), dtype=jnp.float32) * scale_h, 'w_up': jax.random.normal(ks[3], (E, I, H), dtype=jnp.float32) * scale_h, 'w_down': jax.random.normal(ks[4], (E, H, I), dtype=jnp.float32) * scale_i}
    _L0_ffn_in = _L0_ffn_setup()
    _d = {'L0_attn_tokens': _L0_attn_in['tokens'], 'L0_attn_norm_w': _L0_attn_in['norm_w'], 'L0_attn_W_in': _L0_attn_in['W_in'], 'L0_attn_b_in': _L0_attn_in['b_in'], 'L0_attn_W_out': _L0_attn_in['W_out'], 'L0_attn_b_out': _L0_attn_in['b_out'], 'L0_attn_W_skip': _L0_attn_in['W_skip'], 'L0_attn_b_skip': _L0_attn_in['b_skip'], 'L0_attn_log_decay': _L0_attn_in['log_decay'], 'L0_ffn_gate_w': _L0_ffn_in['gate_w'], 'L0_ffn_w_gate': _L0_ffn_in['w_gate'], 'L0_ffn_w_up': _L0_ffn_in['w_up'], 'L0_ffn_w_down': _L0_ffn_in['w_down']}
    _x0 = _d['L0_attn_tokens']
    _d['L0_attn_tokens'] = jax.random.normal(jax.random.fold_in(jax.random.key(seed), 1), (2, 2048, 256), dtype=_x0.dtype)
    del _x0
    return _d

def reference(L0_attn_tokens, L0_attn_norm_w, L0_attn_W_in, L0_attn_b_in, L0_attn_W_out, L0_attn_b_out, L0_attn_W_skip, L0_attn_b_skip, L0_attn_log_decay, L0_ffn_gate_w, L0_ffn_w_gate, L0_ffn_w_up, L0_ffn_w_down):

    def _L0_attn_ref(tokens, norm_w, W_in, b_in, W_out, b_out, W_skip, b_skip, log_decay):
        import jax, jax.numpy as jnp
        import numpy as np
        EPS = 0.0001
        ms = jnp.mean(tokens * tokens, axis=-1, keepdims=True)
        x = tokens * jax.lax.rsqrt(ms + EPS) * norm_w
        decay = jax.nn.sigmoid(log_decay)
        u = jnp.einsum('bsd,nd->bsn', x, W_in) + b_in

        def step(state, u_t):
            state = decay * state + u_t
            return (state, state)
        B, S, _ = x.shape
        init = jnp.zeros((B, W_in.shape[0]), dtype=x.dtype)
        _, states = jax.lax.scan(step, init, jnp.swapaxes(u, 0, 1))
        states = jnp.swapaxes(states, 0, 1)
        y = jnp.einsum('bsn,dn->bsd', states, W_out) + b_out
        y = y + jnp.einsum('bsd,ed->bse', x, W_skip) + b_skip
        return tokens + y

    def _L0_ffn_ref(hidden_states, gate_w, w_gate, w_up, w_down):
        import jax, jax.numpy as jnp
        import numpy as np
        B, S, H, I, E = (2, 1024, 256, 128, 8)
        b, s, h = hidden_states.shape
        x = hidden_states.reshape(-1, h)
        logits = x @ gate_w.T
        top_v = jnp.max(logits, axis=-1)
        sel = jnp.argmax(logits, axis=-1)
        rw = jax.nn.sigmoid(top_v)
        out = jnp.zeros_like(x)
        n_exp = gate_w.shape[0]
        for e in range(n_exp):
            mask = (sel == e).astype(x.dtype)
            xs = x * (rw * mask)[:, None]
            g = xs @ w_gate[e].T
            u = xs @ w_up[e].T
            out = out + u * jax.nn.silu(g) @ w_down[e].T
        return out.reshape(b, s, h)
    x = L0_attn_tokens
    xn = _layernorm(x, axis=-1)
    x = x + _L0_attn_ref(xn, L0_attn_norm_w, L0_attn_W_in, L0_attn_b_in, L0_attn_W_out, L0_attn_b_out, L0_attn_W_skip, L0_attn_b_skip, L0_attn_log_decay) + _L0_ffn_ref(xn, L0_ffn_gate_w, L0_ffn_w_gate, L0_ffn_w_up, L0_ffn_w_down)
    return x

_drawn_inputs = setup_inputs


def setup_inputs(seed=0):
    import zlib

    import numpy as np

    out = dict(_drawn_inputs(seed))
    spreads = {'L0_attn_norm_w': (1.0, 0.2), 'L0_attn_log_decay': (0.0, 0.485)}
    factors = {'L0_attn_b_in': 3.839, 'L0_attn_b_out': 7.522, 'L0_attn_b_skip': 7.031}
    for name, (base, spread) in spreads.items():
        noise = np.random.default_rng([zlib.crc32(name.encode()), seed]).standard_normal(out[name].shape)
        drawn = base * np.exp(spread * noise) if base else spread * noise
        out[name] = jnp.asarray(drawn.astype(out[name].dtype))
    for name, factor in factors.items():
        out[name] = (out[name] * factor).astype(out[name].dtype)
    return out
```

```python
from contextlib import ExitStack

import concourse.bass as bass
import numpy as np
from concourse import mybir

F32 = mybir.dt.float32
F32R = mybir.dt.float32r
BF16 = mybir.dt.bfloat16
I32 = mybir.dt.int32
ALU = mybir.AluOpType
ACT = mybir.ActivationFunctionType
AX = mybir.AxisListType.X

P = 128
LN_EPS = 1e-5
RMS_EPS = 1e-4


def program(nc, tokens, w_tok_t, norm_w, w_out_t, b_in, b_out, b_skip, log_decay, w_gate_up_t, w_down_t, out):
    TOKENS, D = tokens.shape
    BATCHES = 2
    SEQ = TOKENS // BATCHES
    N = w_out_t.shape[0]
    E = w_down_t.shape[1]
    INNER = w_down_t.shape[0]
    DC = D // P
    PROJ = w_tok_t.shape[1]
    STEPS = SEQ // P
    GROUPS = STEPS // 2
    GROUP_TILES = 2 * BATCHES
    REGION = TOKENS + P
    PAD_BLOCK = E * REGION
    ROW = 2 * D + 16
    ID_COL = 2 * D
    FULL_SLOTS = TOKENS // P
    SLOTS = FULL_SLOTS + E
    NO_TOKEN = 1 << 20
    PADS = SLOTS
    assert BATCHES * N == P and INNER == P and DC == 2 and PROJ == D + E + N and SLOTS % 4 == 0

    with ExitStack() as ctx:
        def sb(name, shape, dt=F32):
            return ctx.enter_context(nc.sbuf_tensor(name, shape, dt))

        def sem(name):
            return ctx.enter_context(nc.semaphore(name))

        def sems(name, n):
            return [sem(f"{name}{i}") for i in range(n)]

        table = nc.dram_tensor("expert_rows", [PAD_BLOCK + P, ROW], F32).ap()

        ident = sb("ident", [P, P])
        before = sb("before", [P, P], BF16)
        ones = sb("ones", [P, P], BF16)
        rev = sb("rev", [P, E])
        ebase = sb("ebase", [P, E])
        ones_e = sb("ones_e", [P, E])
        restart = sb("restart", [P, E, GROUP_TILES + 1], BF16)
        slot_no = sb("slot_no", [P, FULL_SLOTS])
        slot_row = sb("slot_row", [P, FULL_SLOTS])
        token_ids = sb("token_ids", [P, GROUPS * GROUP_TILES], I32)
        minus_half = sb("minus_half", [P, 2 * GROUP_TILES])
        pad_rows = sb("pad_rows", [P, ROW])
        w_tok = sb("w_tok", [P, DC, PROJ])
        nw = sb("nw", [P, DC])
        w_out = [sb(f"w_out{b}", [P, D]) for b in range(BATCHES)]
        bias_in = sb("bias_in", [64, 2, PROJ])
        bias = sb("bias", [P, PROJ], F32R)
        bias_rows = sb("bias_rows", [P, P], F32R)
        decay = sb("decay", [P, 1])
        w_gu = sb("w_gu", [P, E * DC * 2 * INNER])
        w_dn = sb("w_dn", [P, E * D])

        nothing = sb("nothing", [P, 1])
        bias_sum = sb("bias_sum", [64, PROJ])
        bias_high = sb("bias_high", [64, PROJ], F32R)

        x_all = sb("x_all", [P, GROUPS * GROUP_TILES, D])
        stats = [sb(f"stats{h}", [P, GROUP_TILES, 6]) for h in range(2)]
        mean_var = [sb(f"mean_var{h}", [P, GROUP_TILES, 2]) for h in range(2)]
        pow_in = [sb(f"pow_in{h}", [P, 2, GROUP_TILES]) for h in range(2)]
        pow_out = [sb(f"pow_out{h}", [P, 2, GROUP_TILES]) for h in range(2)]
        res_scale = [sb(f"res_scale{h}", [P, GROUP_TILES]) for h in range(2)]
        res_bias = [sb(f"res_bias{h}", [P, GROUP_TILES]) for h in range(2)]
        inv_rms = [sb(f"inv_rms{h}", [P, GROUP_TILES]) for h in range(2)]
        xr = [sb(f"xr{h}", [P, GROUP_TILES, D]) for h in range(2)]
        xT = [sb(f"xT{k}", [P, DC, BATCHES, P]) for k in range(2)]
        logits = [sb(f"logits{h}", [P, GROUP_TILES, E]) for h in range(2)]
        inputs = [sb(f"inputs{h}", [P, GROUP_TILES, N]) for h in range(2)]
        state = [sb(f"state{k}", [P, P]) for k in range(2)]
        res = [sb(f"res{h}", [P, GROUP_TILES, D]) for h in range(2)]
        row = [sb(f"row{h}", [P, GROUP_TILES, ROW]) for h in range(2)]
        top = sb("top", [P, GROUP_TILES])
        top_true = sb("top_true", [P, GROUP_TILES])
        tanh_top = sb("tanh_top", [P, GROUP_TILES])
        weight = sb("weight", [P, GROUP_TILES])
        xs_scale = sb("xs_scale", [P, GROUP_TILES])
        is_top = sb("is_top", [P, GROUP_TILES, E])
        cand = sb("cand", [P, GROUP_TILES, E])
        first = sb("first", [P, GROUP_TILES])
        chosen = sb("chosen", [P, E, GROUP_TILES + 1], BF16)
        counted = sb("counted", [P, E, GROUP_TILES + 1], BF16)
        at_all = sb("at_all", [P, E, GROUP_TILES])
        at_own = sb("at_own", [P, E, GROUP_TILES])
        place_f = sb("place_f", [P, GROUP_TILES])
        place = [sb(f"place{h}", [P, GROUP_TILES], I32) for h in range(2)]

        count = sb("count", [P, E])
        count_i = sb("count_i", [P, E], I32)
        full_i = sb("full_i", [P, E], I32)
        full = sb("full", [P, E])
        full_end = sb("full_end", [P, E])
        done_e = sb("done_e", [P, FULL_SLOTS, E])
        done_f = sb("done_f", [P, FULL_SLOTS, E])
        slot_e = sb("slot_e", [P, FULL_SLOTS])
        slot_f = sb("slot_f", [P, FULL_SLOTS])
        slot_a = sb("slot_a", [P, FULL_SLOTS])
        slot_b = sb("slot_b", [P, FULL_SLOTS])
        first_row = sb("first_row", [P, SLOTS + E], I32)
        expert_of = sb("expert_of", [P, SLOTS], I32)

        block_in = [sb(f"block_in{u}", [P, ROW]) for u in range(4)]
        bT = [sb(f"bT{u}", [P, DC * P]) for u in range(2)]
        silu = [sb(f"silu{u}", [P, INNER]) for u in range(2)]
        act = [sb(f"act{u}", [P, INNER]) for u in range(2)]
        aT = [sb(f"aT{u}", [P, P]) for u in range(2)]
        result = [sb(f"result{u}", [P, D]) for u in range(4)]

        banks = ctx.enter_context(nc.psum_tensor("banks", [P, 8, 512], F32))
        bank = [banks[:, i, :] for i in range(8)]
        ps_xT = bank[0:2]
        ps_y = bank[2:6]
        ps_uT = bank[6]
        ps_rank = bank[7]
        ps_bT, ps_gu, ps_aT, ps_dn = bank[0:2], bank[2:4], bank[4:6], bank[6:8]

        s_x = sems("x_loaded", 2)
        s_wtok, s_wout, s_bias, s_nw, s_decay, s_wgu, s_wdn = (
            sem(f"{n}_loaded") for n in ("w_tok", "w_out", "bias", "norm_w", "decay", "w_gate_up", "w_down"))
        s_set = sem("pool_setup")
        s_const = sem("constants_ready")
        s_wready = sem("weights_ready")
        s_adecay = sem("decay_tanh")
        s_stats = sem("stats_ready")
        s_pow = sem("powers_ready")
        s_coef = sem("coefficients_ready")
        s_xr = sem("normalised_ready")
        s_psxT = sem("transposed_in_psum")
        s_xT = sem("transposed_ready")
        s_y = sem("projected")
        s_lu = sem("logits_and_inputs_ready")
        s_uT = sem("inputs_transposed")
        s_scan = sem("states_ready")
        s_wo = sem("states_projected")
        s_base = sem("base_ready")
        s_res = sem("residual_ready")
        s_top = sem("top_ready")
        s_tanh = sem("tanh_ready")
        s_xss = sem("row_scale_ready")
        s_xs = sem("scaled_rows_ready")
        s_ch = sem("chosen_ready")
        s_rank = sem("ranks_ready")
        s_go = sem("pool_goes_on")
        s_place = sem("places_ready")
        s_sent = sems("rows_sent", 2)
        s_free = sem("rows_free")
        s_v = sem("vector_order")
        s_cnt = sem("counts_in_psum")
        s_tab = sem("slot_tables_ready")
        s_padblk = sem("pad_block_written")
        s_pad = sem("padding_written")
        s_in = sems("block_loaded", 4)
        s_psbT = sem("block_transposed_in_psum")
        s_bT = sem("block_transposed")
        s_gu = sem("gate_up_ready")
        s_silu = sem("silu_ready")
        s_act = sem("act_ready")
        s_psaT = sem("act_transposed_in_psum")
        s_aT = sem("act_transposed")
        s_dn = sem("down_ready")
        s_r = sem("result_ready")
        s_out = sems("result_sent", 4)

        block = ctx.enter_context(nc.Block())

        SPARE_Y = 2 * BATCHES
        SPARE_XT = 2
        SPARE_SCAN = 1
        SPARE_BASE = 2 * BATCHES
        SPARE_XS = 2
        SPARE_FREE = 2
        SPARE_RING = 2

        LOOPED = GROUPS // 2 - 1
        STEP_COUNT = 13

        def over_groups(eng, body):
            with eng.Fori(0, LOOPED) as it:
                for h in range(2):
                    body(it * 2 + h, it, h, 2)
            for h in range(2):
                body(2 * LOOPED + h, LOOPED, h, 1 - h)

        def over_blocks(eng, stages):
            most = max(lead for lead, _ in stages)
            for j in range(-most, 0):
                for lead, step in stages:
                    if j + lead >= 0:
                        step(0, j + lead)
            with eng.Fori(0, SLOTS // 4 - 1) as i:
                for u in range(4):
                    for lead, step in stages:
                        step(i, u + lead)
            for u in range(4):
                for lead, step in stages:
                    if u + lead < 4:
                        step(SLOTS // 4 - 1, u + lead)

        @block.sync
        def _(sp):
            def load_x(g, it, h, last):
                sp.wait_ge(s_x[h], 32 * it)
                for b in range(BATCHES):
                    src = tokens[bass.ds(g * 2 * P + b * SEQ, 2 * P), :].rearrange("(k p) d -> p k d", p=P)
                    dst = x_all[:, bass.ds(g * GROUP_TILES, GROUP_TILES), :].rearrange(
                        "p (k b) d -> p b k d", b=BATCHES)[:, b]
                    sp.dma_start(dst, src).then_inc(s_x[h], 16)

            def load_x0(h):
                for b in range(BATCHES):
                    src = tokens[h * 2 * P + b * SEQ:(h + 1) * 2 * P + b * SEQ, :].rearrange("(k p) d -> p k d", p=P)
                    dst = x_all[:, h * GROUP_TILES:(h + 1) * GROUP_TILES, :].rearrange(
                        "p (k b) d -> p b k d", b=BATCHES)[:, b]
                    sp.dma_start(dst, src).then_inc(s_x[h], 16)

            sp.sem_inc(s_free, SPARE_FREE)
            load_x0(0)
            sp.dma_start(w_tok[:, :, :], w_tok_t.rearrange("(c p) n -> p c n", p=P)).then_inc(s_wtok, 16)
            sp.dma_start(nw[:, :], norm_w).then_inc(s_nw, 16)
            load_x0(1)
            for b in range(BATCHES):
                sp.dma_start(w_out[b][b * N:(b + 1) * N, :], w_out_t).then_inc(s_wout, 16)
            with sp.Fori(1, GROUPS // 2) as it:
                for h in range(2):
                    load_x(it * 2 + h, it, h, False)
            sp.dma_start(w_gu[:, :], w_gate_up_t.rearrange("p e n -> p (e n)")).then_inc(s_wgu, 16)
            sp.dma_start(w_dn[:, :], w_down_t.rearrange("p e n -> p (e n)")).then_inc(s_wdn, 16)
            sp.wait_ge(s_const, 2)
            sp.dma_start(table[PAD_BLOCK:PAD_BLOCK + P, :], pad_rows[:, :]).then_inc(s_padblk, 16)

            def rows_sent(g, it, h, left):
                if left == 2:
                    sp.wait_ge(s_sent[h], (it + 1) * 16 * GROUP_TILES)
                    sp.sem_inc(s_free, 1)

            over_groups(sp, rows_sent)

            sp.wait_ge(s_tab, 1)
            for e in range(E):
                r = sp.value_load(first_row[0:1, PADS + e:PADS + e + 1], min_val=0, max_val=PAD_BLOCK)
                sp.dma_start(table[bass.ds(r, P), :], pad_rows[:, :]).then_inc(s_pad, 16)
            for h in range(2):
                sp.wait_ge(s_sent[h], 16 * GROUP_TILES * (GROUPS // 2))
            sp.wait_ge(s_padblk, 16)

            def load_blocks(i):
                for u in range(4):
                    r = sp.value_load(first_row[0:1, bass.ds(i * 4 + u, 1)], min_val=0, max_val=PAD_BLOCK)
                    if not isinstance(i, int):
                        sp.wait_ge(s_out[u], i * 16)
                    sp.dma_start(block_in[u][:, :], table[bass.ds(r, P), :]).then_inc(s_in[u], 16)

            load_blocks(0)
            with sp.Fori(1, FULL_SLOTS // 4) as i:
                load_blocks(i)
            sp.wait_ge(s_pad, 16 * E)
            with sp.Fori(FULL_SLOTS // 4, SLOTS // 4) as i:
                load_blocks(i)
            for u in range(4):
                sp.wait_ge(s_out[u], 16 * (SLOTS // 4))

        @block.gpsimd
        def _(pool):
            pool.memset(minus_half[:, :], -0.5).then_inc(s_set, 1)
            pool.memset(ident[:, :], 0.0).then_inc(s_set, 1)
            pool.memset(before[:, :], 1.0).then_inc(s_set, 1)
            pool.wait_ge(s_set, 3)
            pool.affine_select(out=ident[:, :], in_=ident[:, :], compare_op=ALU.not_equal, fill=1.0, base=0,
                               pattern=[[-1, P]], channel_multiplier=1).then_inc(s_set, 1)
            pool.affine_select(out=before[:, :], in_=before[:, :], compare_op=ALU.is_gt, fill=0.0, base=0,
                               pattern=[[1, P]], channel_multiplier=-1).then_inc(s_set, 1)
            pool.memset(ones[:, :], 1.0)
            pool.memset(bias_in[:, :, :], 0.0)
            pool.memset(ones_e[:, :], 1.0)
            pool.wait_ge(s_set, 5)
            pool.memset(state[1][:, P - 1:P], 0.0)
            pool.memset(restart[:, :, 1:], 1.0)
            pool.memset(restart[:, :, 0:1], 0.0)
            pool.memset(counted[:, :, GROUP_TILES:], 0.0)
            iota = dict(allow_small_or_imprecise_dtypes=True)
            pool.iota(rev[:, :], pattern=[[-1, E]], base=E, channel_multiplier=0, **iota)
            pool.iota(ebase[:, :], pattern=[[REGION, E]], base=0, channel_multiplier=0, **iota)
            pool.iota(token_ids[:, :], pattern=[[2 * P, GROUPS], [P, 2], [SEQ, BATCHES]], base=0,
                      channel_multiplier=1)
            for h in range(2):
                pool.memset(row[h][:, :, ID_COL + 1:ROW], 0.0)
            pool.iota(slot_no[:, :], pattern=[[1, FULL_SLOTS]], base=0, channel_multiplier=0, **iota)
            pool.iota(slot_row[:, :], pattern=[[P, FULL_SLOTS]], base=0, channel_multiplier=0, **iota)
            pool.iota(expert_of[:, FULL_SLOTS:SLOTS], pattern=[[1, E]], base=0, channel_multiplier=0).then_inc(s_const, 1)
            pool.memset(pad_rows[:, 0:ID_COL], 0.0)
            pool.memset(pad_rows[:, ID_COL:ROW].bitcast(I32), NO_TOKEN).then_inc(s_const, 1)

            def powers(g, h):
                pool.wait_ge(s_stats, g + 1)
                pool.tensor_tensor(pow_out[h][:, :, :], pow_in[h][:, :, :],
                                   minus_half[:, :].rearrange("p (a t) -> p a t", a=2), ALU.pow).then_inc(s_pow, 1)

            powers(0, 0)
            powers(1, 1)

            def group(g, it, h, left):
                if left == 2:
                    powers(g + 2, h)
                pool.wait_ge(s_place, g + 1)
                pool.wait_ge(s_xs, g + 1 + SPARE_XS)
                pool.wait_ge(s_base, (g + 1) * GROUP_TILES + SPARE_BASE)
                pool.sem_inc(s_go, 1)
                for t in range(GROUP_TILES):
                    pool.indirect_dma_start(table, bass.IndirectOffsetOnAxis(place[h][:, t:t + 1], 0),
                                            row[h][:, t, :], None).then_inc(s_sent[h], 16)

            over_groups(pool, group)

            def send(i, u):
                pool.wait_ge(s_r, i * 4 + u + 1 + SPARE_RING)
                pool.sem_inc(s_go, 1)
                pool.indirect_dma_start(
                    out, bass.IndirectOffsetOnAxis(block_in[u][:, ID_COL:ID_COL + 1].bitcast(I32), 0),
                    result[u][:, :], None, bounds_check=TOKENS - 1, oob_is_err=False).then_inc(s_out[u], 16)

            with pool.Fori(0, SLOTS // 4) as i:
                for u in range(4):
                    send(i, u)

        @block.scalar
        def _(a):
            a.dma_start(decay[0:N, :], log_decay.rearrange("(n o) -> n o", o=1)).then_inc(s_decay, 16)
            a.dma_start(decay[N:2 * N, :], log_decay.rearrange("(n o) -> n o", o=1)).then_inc(s_decay, 16)
            one_row = lambda v: v.rearrange("(o n) -> o n", o=1)
            a.wait_ge(s_const, 1)
            for r in (0, 32):
                a.dma_start(bias_in[r:r + 1, 0, 0:D], one_row(b_out)).then_inc(s_bias, 16)
                a.dma_start(bias_in[r:r + 1, 1, 0:D], one_row(b_skip)).then_inc(s_bias, 16)
                a.dma_start(bias_in[r:r + 1, 0, D + E:PROJ], one_row(b_in)).then_inc(s_bias, 16)
            a.wait_ge(s_decay, 32)
            a.activation(decay[:, :], decay[:, :], ACT.Tanh, scale=0.5).then_inc(s_adecay, 1)

            a.sem_inc(s_xT, SPARE_XT)
            a.sem_inc(s_xs, SPARE_XS)
            a.sem_inc(s_bT, SPARE_RING)
            a.sem_inc(s_aT, SPARE_RING)

            def copy_xT(s, k):
                a.wait_ge(s_psxT, s + 1)
                a.wait_ge(s_y, (s - 1) * BATCHES + SPARE_Y)
                a.activation(xT[k][:, :, :, :].rearrange("p c b n -> p (c b n)"), ps_xT[k][:, :],
                             ACT.Copy).then_inc(s_xT, 1)

            def copy_lu(s, h, k):
                a.wait_ge(s_y, (s + 1) * BATCHES + SPARE_Y)
                tiles = slice(BATCHES * k, BATCHES * (k + 1))
                y = banks[:, 2 + 2 * k:4 + 2 * k, :]
                a.activation(logits[h][:, tiles, :], y[:, :, D:D + E], ACT.Copy)
                a.activation(inputs[h][:, tiles, :], y[:, :, D + E:PROJ], ACT.Copy).then_inc(s_lu, 1)

            def residual(g, h):
                a.wait_ge(s_coef, g + 1)
                for t in range(GROUP_TILES):
                    ins = a.activation(res[h][:, t, :], x_all[:, bass.ds(g * GROUP_TILES + t, 1), :].rearrange(
                        "p o d -> p (o d)"), ACT.Identity, bias=res_bias[h][:, t:t + 1],
                        scale=res_scale[h][:, t:t + 1])
                ins.then_inc(s_res, 1)

            copy_xT(0, 0)
            copy_lu(0, 0, 0)

            def group(g, it, h, left):
                copy_xT(g * 2 + 1, 1)
                residual(g, h)
                copy_lu(g * 2 + 1, h, 1)
                if left:
                    copy_xT(g * 2 + 2, 0)
                a.wait_ge(s_top, g + 1)
                a.activation(tanh_top[:, :], top_true[:, :], ACT.Tanh, scale=0.5).then_inc(s_tanh, 1)
                a.wait_ge(s_xss, g + 1)
                a.wait_ge(s_free, g - 1 + SPARE_FREE)
                for t in range(GROUP_TILES):
                    ins = a.activation(row[h][:, t, 0:D], xr[h][:, t, :], ACT.Copy, scale=xs_scale[:, t:t + 1])
                ins.then_inc(s_xs, 1)
                if left:
                    copy_lu(g * 2 + 2, 1 - h, 0)

            over_groups(a, group)

            def copy_bT(i, u):
                a.wait_ge(s_psbT, i * 4 + u + 1)
                a.wait_ge(s_gu, i * 4 + u - 1 + SPARE_RING)
                a.activation(bT[u % 2][:, :], ps_bT[u % 2][:, 0:DC * P], ACT.Copy).then_inc(s_bT, 1)

            def gate(i, u):
                a.wait_ge(s_gu, i * 4 + u + 1 + SPARE_RING)
                a.wait_ge(s_act, i * 4 + u - 1 + SPARE_RING)
                a.activation(silu[u % 2][:, :], ps_gu[u % 2][:, 0:INNER], ACT.Silu).then_inc(s_silu, 1)

            def copy_aT(i, u):
                a.wait_ge(s_psaT, i * 4 + u + 1)
                a.wait_ge(s_dn, i * 4 + u - 1 + SPARE_RING)
                a.activation(aT[u % 2][:, :], ps_aT[u % 2][:, 0:P], ACT.Copy).then_inc(s_aT, 1)

            over_blocks(a, [(3, copy_bT), (2, gate), (1, copy_aT)])

        @block.tensor
        def _(pe):
            pe.sem_inc(s_y, SPARE_Y)
            pe.sem_inc(s_gu, SPARE_RING)
            pe.sem_inc(s_dn, SPARE_RING)

            def transpose_x(s, h, k):
                pe.wait_ge(s_xr, s + 1)
                pe.wait_ge(s_xT, s - 1 + SPARE_XT)
                for c in range(DC):
                    for b in range(BATCHES):
                        ins = pe.transpose(ps_xT[k][:, (c * BATCHES + b) * P:(c * BATCHES + b + 1) * P],
                                           xr[h][:, 2 * k + b, c * P:(c + 1) * P], ident[:, :])
                ins.then_inc(s_psxT, 1)

            def project(s, k):
                pe.wait_ge(s_xT, s + 1 + SPARE_XT)
                for b in range(BATCHES):
                    pe.wait_ge(s_base, (s - 2) * BATCHES + b + 1 + SPARE_BASE)
                    y = ps_y[2 * k + b][:, 0:PROJ]
                    pe.matmul(y, bias_rows[:, :], bias[:, :], start=True, stop=False)
                    for c in range(DC):
                        ins = pe.matmul(y, xT[k][:, c, b, :], w_tok[:, c, :], start=False, stop=(c == DC - 1))
                    ins.then_inc(s_y, 1)

            def transpose_u(s, h, k):
                pe.wait_ge(s_lu, s + 1)
                pe.wait_ge(s_scan, s + SPARE_SCAN)
                pe.transpose(ps_uT[:, 0:P], inputs[h][:, 2 * k:2 * k + 2, :].rearrange("p b n -> p (b n)"), ident[:, :]).then_inc(s_uT, 1)

            def project_states(s, k):
                pe.wait_ge(s_scan, s + 1 + SPARE_SCAN)
                for b in range(BATCHES):
                    pe.matmul(ps_y[2 * k + b][:, 0:D], state[k][:, :], w_out[b][:, :], start=False, stop=True,
                              skip_group_check=True).then_inc(s_wo, 1)

            pe.wait_ge(s_const, 1)
            transpose_x(0, 0, 0)
            pe.wait_ge(s_wready, 1)
            pe.wait_ge(s_wout, 16 * BATCHES)
            project(0, 0)

            def group(g, it, h, left):
                transpose_x(g * 2 + 1, h, 1)
                transpose_u(g * 2, h, 0)
                project(g * 2 + 1, 1)
                project_states(g * 2, 0)
                if left:
                    transpose_x(g * 2 + 2, 1 - h, 0)
                transpose_u(g * 2 + 1, h, 1)
                if left:
                    project(g * 2 + 2, 0)
                pe.wait_ge(s_ch, g + 1)
                ranks = ps_rank[:, 0:E * GROUP_TILES].rearrange("p (e t) -> p e t", e=E)
                pe.matmul(ranks, before[:, :], chosen[:, :, 1:], start=True, stop=False)
                pe.matmul(ranks, ones[:, :], counted[:, :, 0:GROUP_TILES], start=False, stop=True).then_inc(s_rank, 1)
                project_states(g * 2 + 1, 1)

            over_groups(pe, group)
            pe.wait_ge(s_place, GROUPS)
            pe.matmul(ps_rank[:, 0:E], ones[:, :], counted[:, :, GROUP_TILES], start=True, stop=True).then_inc(s_cnt, 1)

            pe.wait_ge(s_tab, 1)
            pe.wait_ge(s_wgu, 16)
            pe.wait_ge(s_wdn, 16)

            def expert(i, u):
                return pe.value_load(expert_of[0:1, bass.ds(i * 4 + u, 1)], min_val=0, max_val=E - 1)

            def transpose_block(i, u):
                pe.wait_ge(s_in[u % 4], i * 16 + (u // 4 + 1) * 16)
                pe.wait_ge(s_bT, i * 4 + u - 1 + SPARE_RING)
                for c in range(DC):
                    ins = pe.transpose(ps_bT[u % 2][:, c * P:(c + 1) * P], block_in[u % 4][:, c * P:(c + 1) * P],
                                       ident[:, :])
                ins.then_inc(s_psbT, 1)

            def gate_up(i, u):
                e = expert(i, u)
                pe.wait_ge(s_bT, i * 4 + u + 1 + SPARE_RING)
                pe.wait_ge(s_act, i * 4 + u - 1 + SPARE_RING)
                for c in range(DC):
                    ins = pe.matmul(ps_gu[u % 2][:, 0:2 * INNER], bT[u % 2][:, c * P:(c + 1) * P],
                                    w_gu[:, bass.ds(e * (DC * 2 * INNER) + c * 2 * INNER, 2 * INNER)],
                                    start=(c == 0), stop=(c == DC - 1))
                ins.then_inc(s_gu, 1)

            def transpose_act(i, u):
                pe.wait_ge(s_act, i * 4 + u + 1 + SPARE_RING)
                pe.wait_ge(s_aT, i * 4 + u - 1 + SPARE_RING)
                pe.transpose(ps_aT[u % 2][:, 0:P], act[u % 2][:, :], ident[:, :]).then_inc(s_psaT, 1)

            def down(i, u):
                e = expert(i, u)
                pe.wait_ge(s_aT, i * 4 + u + 1 + SPARE_RING)
                pe.wait_ge(s_r, i * 4 + u - 1 + SPARE_RING)
                pe.matmul(ps_dn[u % 2][:, 0:D], aT[u % 2][:, :], w_dn[:, bass.ds(e * D, D)],
                          start=True, stop=True).then_inc(s_dn, 1)

            over_blocks(pe, [(3, transpose_block), (2, gate_up), (1, transpose_act), (0, down)])

        @block.vector
        def _(v):
            v.sem_inc(s_scan, SPARE_SCAN)
            v.sem_inc(s_base, SPARE_BASE)
            v.sem_inc(s_act, SPARE_RING)
            v.sem_inc(s_r, SPARE_RING)
            step = Step(v, s_v)

            def statistics(g, it, h):
                v.wait_ge(s_x[h], it * 32 + 32)
                for t in range(GROUP_TILES):
                    ins = v.bn_stats(stats[h][:, t, :], x_all[:, bass.ds(g * GROUP_TILES + t, 1), :].rearrange(
                        "p o d -> p (o d)"))
                step(ins)
                v.memset(nothing[:, :], 0.0)
                for t in range(GROUP_TILES):
                    ins = v.bn_aggr(mean_var[h][:, t, :], stats[h][:, t, :])
                step(ins)
                v.tensor_scalar(pow_in[h][:, 0, :], mean_var[h][:, :, 1], 1.0 + RMS_EPS, LN_EPS * RMS_EPS,
                                ALU.mult, ALU.add)
                v.tensor_scalar(pow_in[h][:, 1, :], mean_var[h][:, :, 1], LN_EPS, None, ALU.add).then_inc(s_stats, 1)

            def normalise(g, h):
                v.wait_ge(s_pow, g + 1)
                v.wait_ge(s_xs, g - 1 + SPARE_XS)
                for t in range(GROUP_TILES):
                    ins = v.tensor_scalar(xr[h][:, t, :], x_all[:, bass.ds(g * GROUP_TILES + t, 1), :].rearrange(
                        "p o d -> p (o d)"), mean_var[h][:, t, 0:1], pow_out[h][:, 0, t:t + 1],
                        ALU.subtract, ALU.mult)
                    if t % 2:
                        ins.then_inc(s_xr, 1)
                v.tensor_scalar(res_scale[h][:, :], pow_out[h][:, 1, :], 1.0, None, ALU.add)
                v.scalar_tensor_tensor(res_bias[h][:, :], mean_var[h][:, :, 0], -1.0, pow_out[h][:, 1, :],
                                       ALU.mult, ALU.mult).then_inc(s_coef, 1)
                step(v.tensor_tensor(inv_rms[h][:, :], pow_out[h][:, 0, :], pow_out[h][:, 1, :], ALU.mult))
                step(v.tensor_tensor(inv_rms[h][:, :], inv_rms[h][:, :], pow_in[h][:, 0, :], ALU.mult))

            def scan(s, k):
                v.wait_ge(s_uT, s + 1)
                v.tensor_tensor_scan(state[k][:, :], decay[:, 0:1].to_broadcast([P, P]), ps_uT[:, 0:P],
                                     state[1 - k][:, P - 1:P], ALU.mult, ALU.add).then_inc(s_scan, 1)

            def add_residual(g, it, h, k):
                if k == 0:
                    v.wait_ge(s_res, g + 1)
                    v.wait_ge(s_free, g - 1 + SPARE_FREE)
                    v.tensor_copy(row[h][:, :, ID_COL].bitcast(I32),
                                  token_ids[:, bass.ds(g * GROUP_TILES, GROUP_TILES)])
                for b in range(BATCHES):
                    v.wait_ge(s_wo, (g * 2 + k) * BATCHES + b + 1)
                    v.tensor_tensor(row[h][:, 2 * k + b, D:2 * D], ps_y[2 * k + b][:, 0:D], res[h][:, 2 * k + b, :],
                                    ALU.add).then_inc(s_base, 1)

            def choose(g, h):
                by_tile = [P, GROUP_TILES, E]
                step(v.tensor_reduce(top[:, :], logits[h][:, :, :], AX, ALU.max))
                v.tensor_tensor(top_true[:, :], top[:, :], inv_rms[h][:, :], ALU.mult).then_inc(s_top, 1)
                step(v.tensor_tensor(is_top[:, :, :], logits[h][:, :, :], top[:, :].unsqueeze(2).to_broadcast(by_tile), ALU.is_ge))
                step(v.tensor_tensor(cand[:, :, :], is_top[:, :, :], rev[:, :].unsqueeze(1).to_broadcast(by_tile),
                                     ALU.mult))
                step(v.tensor_reduce(first[:, :], cand[:, :, :], AX, ALU.max))
                v.tensor_copy(chosen[:, :, 0:1], counted[:, :, GROUP_TILES:])
                step(v.tensor_tensor(chosen[:, :, 1:].rearrange("p e t -> p t e"),
                                     rev[:, :].unsqueeze(1).to_broadcast(by_tile),
                                     first[:, :].unsqueeze(2).to_broadcast(by_tile), ALU.is_equal))
                v.tensor_tensor_scan(counted[:, :, :].rearrange("p e t -> p (e t)"),
                                     restart[:, :, :].rearrange("p e t -> p (e t)"),
                                     chosen[:, :, :].rearrange("p e t -> p (e t)"), 0.0,
                                     ALU.mult, ALU.add).then_inc(s_ch, 1)

            def scale_of_rows(g, h):
                v.wait_ge(s_tanh, g + 1)
                step(v.tensor_scalar(weight[:, :], tanh_top[:, :], 0.5, 0.5, ALU.mult, ALU.add))
                v.tensor_tensor(xs_scale[:, :], weight[:, :], inv_rms[h][:, :], ALU.mult).then_inc(s_xss, 1)

            def places(g, h):
                v.wait_ge(s_rank, g + 1)
                step(v.tensor_tensor(at_all[:, :, :], ps_rank[:, 0:E * GROUP_TILES].rearrange("p (e t) -> p e t", e=E),
                                     ebase[:, :].unsqueeze(2).to_broadcast([P, E, GROUP_TILES]), ALU.add))
                step(v.tensor_tensor(at_own[:, :, :], at_all[:, :, :], chosen[:, :, 1:], ALU.mult))
                step(v.tensor_reduce(place_f[:, :], at_own[:, :, :].rearrange("p e t -> p t e"), AX, ALU.add))
                v.tensor_copy(place[h][:, :], place_f[:, :]).then_inc(s_place, 1)

            for b in range(BATCHES):
                v.memset(w_out[b][(1 - b) * N:(2 - b) * N, :], 0.0)
            v.memset(bias[:, :].bitcast(F32), 0.0)
            step(v.memset(bias_rows[:, :].bitcast(F32), 0.0))
            v.memset(bias_rows[0:1, :].bitcast(F32), 1.0)
            v.memset(bias_rows[32:33, :].bitcast(F32), 1.0)
            v.wait_ge(s_wtok, 16)
            v.wait_ge(s_nw, 16)
            for c in range(DC):
                for lo, hi in ((0, D), (D + E, PROJ)):
                    v.tensor_scalar(w_tok[:, c, lo:hi], w_tok[:, c, lo:hi], nw[:, c:c + 1], None, ALU.mult)
            v.wait_ge(s_const, 1)
            v.wait_ge(s_bias, 16 * 6)
            step(v.tensor_tensor(bias_sum[:, :], bias_in[:, 0, :], bias_in[:, 1, :], ALU.add))
            v.tensor_copy(bias[0:1, :], bias_sum[0:1, :])
            step(v.tensor_copy(bias_high[32:33, :], bias_sum[32:33, :]))
            v.tensor_tensor(bias[32:33, :], bias_sum[32:33, :], bias_high[32:33, :].bitcast(F32), ALU.subtract)
            v.wait_ge(s_adecay, 1)
            step(v.tensor_scalar(decay[:, :], decay[:, :], 0.5, 0.5, ALU.mult, ALU.add))
            v.memset(nothing[:, :], 0.0).then_inc(s_wready, 1)
            statistics(0, 0, 0)
            statistics(1, 0, 1)
            normalise(0, 0)
            before_groups = step.n

            def group(g, it, h, left):
                step.begin(g * STEP_COUNT + before_groups)
                scan(g * 2, 0)
                if left:
                    normalise(g + 1, 1 - h)
                add_residual(g, it, h, 0)
                scan(g * 2 + 1, 1)
                choose(g, h)
                scale_of_rows(g, h)
                if left == 2:
                    statistics(g + 2, it + 1, h)
                places(g, h)
                add_residual(g, it, h, 1)
                assert left < 2 or step.n == STEP_COUNT, step.n
                step.skip(STEP_COUNT)

            over_groups(v, group)
            step.begin(GROUPS * STEP_COUNT + before_groups)

            v.wait_ge(s_cnt, 1)
            step(v.tensor_copy(count[:, :], ps_rank[:, 0:E]))
            v.tensor_tensor(first_row[:, PADS:PADS + E], count[:, :], ebase[:, :], ALU.add)
            step(v.tensor_copy(count_i[:, :], count[:, :]))
            step(v.tensor_scalar(full_i[:, :], count_i[:, :], 7, None, ALU.arith_shift_right))
            step(v.tensor_copy(full[:, :], full_i[:, :]))
            v.scalar_tensor_tensor(first_row[:, FULL_SLOTS:SLOTS], full[:, :], float(P), ebase[:, :], ALU.mult, ALU.add)
            step(v.tensor_tensor_scan(full_end[:, :], ones_e[:, :], full[:, :], 0.0, ALU.mult, ALU.add))
            by_slot = [P, FULL_SLOTS, E]
            step(v.tensor_tensor(done_e[:, :, :], slot_no[:, :].unsqueeze(2).to_broadcast(by_slot),
                                 full_end[:, :].unsqueeze(1).to_broadcast(by_slot), ALU.is_ge))
            v.tensor_reduce(slot_e[:, :], done_e[:, :, :], AX, ALU.add)
            step(v.tensor_tensor(done_f[:, :, :], done_e[:, :, :], full[:, :].unsqueeze(1).to_broadcast(by_slot),
                                 ALU.mult))
            v.scalar_tensor_tensor(slot_a[:, :], slot_e[:, :], float(REGION), slot_row[:, :], ALU.mult, ALU.add)
            step(v.tensor_reduce(slot_f[:, :], done_f[:, :, :], AX, ALU.add))
            v.tensor_scalar(expert_of[:, 0:FULL_SLOTS], slot_e[:, :], float(E - 1), None, ALU.min)
            step(v.scalar_tensor_tensor(slot_b[:, :], slot_f[:, :], -float(P), slot_a[:, :], ALU.mult, ALU.add))
            v.tensor_scalar(first_row[:, 0:FULL_SLOTS], slot_b[:, :], float(PAD_BLOCK), None,
                            ALU.min).then_inc(s_tab, 1)

            def product(i, u):
                v.wait_ge(s_silu, i * 4 + u + 1)
                v.tensor_tensor(act[u % 2][:, :], ps_gu[u % 2][:, INNER:2 * INNER], silu[u % 2][:, :],
                                ALU.mult).then_inc(s_act, 1)

            def add_terms(i, u):
                v.wait_ge(s_dn, i * 4 + u + 1 + SPARE_RING)
                v.tensor_tensor(result[u % 4][:, :], ps_dn[u % 2][:, 0:D], block_in[u % 4][:, D:2 * D],
                                ALU.add).then_inc(s_r, 1)

            over_blocks(v, [(2, product), (0, add_terms)])


class Step:

    def __init__(self, eng, sem):
        self.eng, self.sem, self.base, self.n = eng, sem, 0, 0

    def begin(self, base):
        self.base, self.n = base, 0

    def __call__(self, ins):
        ins.then_inc(self.sem, 1)
        self.n += 1
        self.eng.wait_ge(self.sem, self.base + self.n)

    def skip(self, n):
        if self.n < n:
            self.eng.sem_inc(self.sem, n - self.n)


def kernel(L0_attn_tokens, L0_attn_norm_w, L0_attn_W_in, L0_attn_b_in, L0_attn_W_out, L0_attn_b_out,
           L0_attn_W_skip, L0_attn_b_skip, L0_attn_log_decay, L0_ffn_gate_w, L0_ffn_w_gate, L0_ffn_w_up,
           L0_ffn_w_down):
    import concourse.bacc as bacc
    from concourse.bass_utils import run_bass_kernel_spmd

    B, S, D = L0_attn_tokens.shape
    E, I, _ = L0_ffn_w_gate.shape
    w_tok = np.concatenate([np.asarray(w).T for w in (L0_attn_W_skip, L0_ffn_gate_w, L0_attn_W_in)], axis=1)
    w_gu = np.stack([np.asarray(L0_ffn_w_gate), np.asarray(L0_ffn_w_up)], axis=1)
    w_gu = w_gu.reshape(E, 2, I, D // P, P).transpose(4, 0, 3, 1, 2).reshape(P, E, -1)
    arrays = {
        "tokens": np.asarray(L0_attn_tokens).reshape(B * S, D),
        "w_tok_t": w_tok,
        "norm_w": np.asarray(L0_attn_norm_w).reshape(D // P, P).T,
        "w_out_t": np.asarray(L0_attn_W_out).T,
        "b_in": L0_attn_b_in,
        "b_out": L0_attn_b_out,
        "b_skip": L0_attn_b_skip,
        "log_decay": L0_attn_log_decay,
        "w_gate_up_t": w_gu,
        "w_down_t": np.asarray(L0_ffn_w_down).transpose(2, 0, 1),
    }
    arrays = {name: np.ascontiguousarray(a) for name, a in arrays.items()}
    nc = bacc.Bacc("TRN2", target_bir_lowering=False, num_devices=1)
    args = {name: nc.dram_tensor(name, a.shape, F32, kind="ExternalInput").ap() for name, a in arrays.items()}
    out = nc.dram_tensor("out", (B * S, D), F32, kind="ExternalOutput").ap()
    program(nc, **args, out=out)
    r = run_bass_kernel_spmd(nc, [arrays], core_ids=[0])
    return r.results[0]["out"].reshape(B, S, D)
```

```python
from contextlib import ExitStack

import concourse.bass as bass
import numpy as np
from concourse import mybir

F32 = mybir.dt.float32
F32R = mybir.dt.float32r
BF16 = mybir.dt.bfloat16
I32 = mybir.dt.int32
ALU = mybir.AluOpType
ACT = mybir.ActivationFunctionType
AX = mybir.AxisListType.X

P = 128
LN_EPS = 1e-5
RMS_EPS = 1e-4


def program(nc, tokens, w_tok_t, norm_w, w_out_t, b_in, b_out, b_skip, log_decay, w_gate_up_t, w_down_t, out):
    TOKENS, D = tokens.shape
    BATCHES = 2
    SEQ = TOKENS // BATCHES
    N = w_out_t.shape[0]
    E = w_down_t.shape[1]
    INNER = w_down_t.shape[0]
    DC = D // P
    PROJ = w_tok_t.shape[1]
    STEPS = SEQ // P
    GROUPS = STEPS // 2
    GROUP_TILES = 2 * BATCHES
    REGION = TOKENS + P
    PAD_BLOCK = E * REGION
    ROW = 2 * D + 16
    ID_COL = 2 * D
    FULL_SLOTS = TOKENS // P
    SLOTS = FULL_SLOTS + E
    RING = 8
    NO_TOKEN = 1 << 20
    PADS = SLOTS
    assert BATCHES * N == P and INNER == P and DC == 2 and PROJ == D + E + N and FULL_SLOTS % RING == 0 and E % RING == 0

    with ExitStack() as ctx:
        def sb(name, shape, dt=F32):
            return ctx.enter_context(nc.sbuf_tensor(name, shape, dt))

        def sem(name):
            return ctx.enter_context(nc.semaphore(name))

        def sems(name, n):
            return [sem(f"{name}{i}") for i in range(n)]

        table = nc.dram_tensor("expert_rows", [PAD_BLOCK + P, ROW], F32).ap()

        ident = sb("ident", [P, P])
        before = sb("before", [P, P], BF16)
        ones = sb("ones", [P, P], BF16)
        rev = sb("rev", [P, E])
        ebase = sb("ebase", [P, E])
        ones_e = sb("ones_e", [P, E])
        restart = sb("restart", [P, E, GROUP_TILES + 1], BF16)
        slot_no = sb("slot_no", [P, FULL_SLOTS])
        slot_row = sb("slot_row", [P, FULL_SLOTS])
        token_ids = sb("token_ids", [P, GROUPS * GROUP_TILES], I32)
        minus_half = sb("minus_half", [P, 2 * GROUP_TILES])
        pad_rows = sb("pad_rows", [P, ROW])
        w_tok = sb("w_tok", [P, DC, PROJ])
        nw = sb("nw", [P, DC])
        w_out = [sb(f"w_out{b}", [P, D]) for b in range(BATCHES)]
        bias_in = sb("bias_in", [P, PROJ])
        bias = sb("bias", [P, PROJ], F32R)
        ones_r = sb("ones_r", [P, P], F32R)
        decay = sb("decay", [P, 1])
        w_gu = sb("w_gu", [P, E * DC * 2 * INNER])
        w_dn = sb("w_dn", [P, E * D])

        nothing = sb("nothing", [P, 1])
        func_set = sb("func_set", [P, 1])

        x_all = sb("x_all", [P, GROUPS * GROUP_TILES, D])
        stats = [sb(f"stats{h}", [P, GROUP_TILES, 6]) for h in range(2)]
        mean_var = [sb(f"mean_var{h}", [P, GROUP_TILES, 2]) for h in range(2)]
        pow_in = [sb(f"pow_in{h}", [P, 2, GROUP_TILES]) for h in range(2)]
        pow_out = [sb(f"pow_out{h}", [P, 2, GROUP_TILES]) for h in range(2)]
        res_scale = [sb(f"res_scale{h}", [P, GROUP_TILES]) for h in range(2)]
        res_bias = [sb(f"res_bias{h}", [P, GROUP_TILES]) for h in range(2)]
        inv_rms = [sb(f"inv_rms{h}", [P, GROUP_TILES]) for h in range(2)]
        xr = [sb(f"xr{h}", [P, GROUP_TILES, D]) for h in range(2)]
        xT = [sb(f"xT{k}", [P, DC, BATCHES, P]) for k in range(2)]
        logits = [sb(f"logits{h}", [P, GROUP_TILES, E]) for h in range(2)]
        inputs = [sb(f"inputs{h}", [P, GROUP_TILES, N]) for h in range(2)]
        state = [sb(f"state{k}", [P, P]) for k in range(2)]
        res = [sb(f"res{h}", [P, GROUP_TILES, D]) for h in range(2)]
        row = [sb(f"row{h}", [P, GROUP_TILES, ROW]) for h in range(2)]
        top = sb("top", [P, GROUP_TILES])
        top_true = sb("top_true", [P, GROUP_TILES])
        tanh_top = sb("tanh_top", [P, GROUP_TILES])
        weight = sb("weight", [P, GROUP_TILES])
        xs_scale = sb("xs_scale", [P, GROUP_TILES])
        is_top = sb("is_top", [P, GROUP_TILES, E])
        cand = sb("cand", [P, GROUP_TILES, E])
        first = sb("first", [P, GROUP_TILES])
        chosen = sb("chosen", [P, E, GROUP_TILES + 1], BF16)
        counted = sb("counted", [P, E, GROUP_TILES + 1], BF16)
        at_all = sb("at_all", [P, E, GROUP_TILES])
        at_own = sb("at_own", [P, E, GROUP_TILES])
        place_f = sb("place_f", [P, GROUP_TILES])
        place = [sb(f"place{h}", [P, GROUP_TILES], I32) for h in range(2)]

        count = sb("count", [P, E])
        count_i = sb("count_i", [P, E], I32)
        full_i = sb("full_i", [P, E], I32)
        full = sb("full", [P, E])
        full_end = sb("full_end", [P, E])
        done_e = sb("done_e", [P, FULL_SLOTS, E])
        done_f = sb("done_f", [P, FULL_SLOTS, E])
        slot_e = sb("slot_e", [P, FULL_SLOTS])
        slot_f = sb("slot_f", [P, FULL_SLOTS])
        slot_a = sb("slot_a", [P, FULL_SLOTS])
        slot_b = sb("slot_b", [P, FULL_SLOTS])
        first_row = sb("first_row", [P, SLOTS + E], I32)
        expert_of = sb("expert_of", [P, SLOTS], I32)

        block_in = [sb(f"block_in{u}", [P, ROW]) for u in range(RING)]
        bT = [sb(f"bT{u}", [P, DC * P]) for u in range(2)]
        silu = [sb(f"silu{u}", [P, INNER]) for u in range(2)]
        act = [sb(f"act{u}", [P, INNER]) for u in range(2)]
        aT = [sb(f"aT{u}", [P, P]) for u in range(2)]
        result = [sb(f"result{u}", [P, D]) for u in range(RING)]

        banks = ctx.enter_context(nc.psum_tensor("banks", [P, 8, 512], F32))
        bank = [banks[:, i, :] for i in range(8)]
        ps_xT = bank[0:2]
        ps_y = bank[2:6]
        ps_uT = bank[6]
        ps_rank = bank[7]
        ps_bT, ps_gu, ps_aT, ps_dn = bank[0:2], bank[2:4], bank[4:6], bank[6:8]

        s_x = sems("x_loaded", 2)
        s_wtok, s_wout, s_bias, s_nw, s_decay, s_wgu, s_wdn = (
            sem(f"{n}_loaded") for n in ("w_tok", "w_out", "bias", "norm_w", "decay", "w_gate_up", "w_down"))
        s_set = sem("pool_setup")
        s_const = sem("constants_ready")
        s_wready = sem("weights_ready")
        s_bias0 = sem("bias_rows_zeroed")
        s_aset = sem("decay_tanh_and_bias_rounded")
        s_stats = sem("stats_ready")
        s_pow = sem("powers_ready")
        s_coef = sem("coefficients_ready")
        s_xr = sem("normalised_ready")
        s_psxT = sem("transposed_in_psum")
        s_xT = sem("transposed_ready")
        s_y = sem("projected")
        s_lu = sem("logits_and_inputs_ready")
        s_uT = sem("inputs_transposed")
        s_scan = sem("states_ready")
        s_wo = sem("states_projected")
        s_base = sem("base_ready")
        s_res = sem("residual_ready")
        s_top = sem("top_ready")
        s_tanh = sem("tanh_ready")
        s_xss = sem("row_scale_ready")
        s_xs = sem("scaled_rows_ready")
        s_ch = sem("chosen_ready")
        s_rank = sem("ranks_ready")
        s_go = sem("pool_goes_on")
        s_place = sem("places_ready")
        s_sent = sems("rows_sent", 2)
        s_free = sem("rows_free")
        s_v = sem("vector_order")
        s_cnt = sem("counts_in_psum")
        s_tab = sem("slot_tables_ready")
        s_padblk = sem("pad_block_written")
        s_pad = sem("padding_written")
        s_in = sems("block_loaded", RING)
        s_psbT = sem("block_transposed_in_psum")
        s_bT = sem("block_transposed")
        s_gu = sem("gate_up_ready")
        s_silu = sem("silu_ready")
        s_act = sem("act_ready")
        s_psaT = sem("act_transposed_in_psum")
        s_aT = sem("act_transposed")
        s_dn = sem("down_ready")
        s_r = sem("result_ready")
        s_out = sems("result_sent", RING)

        block = ctx.enter_context(nc.Block())

        SPARE_Y = 2 * BATCHES
        SPARE_XT = 2
        SPARE_SCAN = 1
        SPARE_BASE = 2 * BATCHES
        SPARE_XS = 2
        SPARE_FREE = 2
        SPARE_RING = 2

        LOOPED = GROUPS // 2 - 1
        STEP_COUNT = 13

        def over_groups(eng, body):
            with eng.Fori(0, LOOPED) as it:
                for h in range(2):
                    body(it * 2 + h, it, h, 2)
            for h in range(2):
                body(2 * LOOPED + h, LOOPED, h, 1 - h)

        def over_blocks(eng, stages, turn=None):
            most = max(lead for lead, _ in stages)
            if turn:
                turn(0, 2)
            for j in range(-most, 0):
                for lead, step in stages:
                    if j + lead >= 0:
                        step(0, j + lead)
            with eng.Fori(0, SLOTS // RING - 1) as i:
                if turn:
                    turn(i, RING + 2)
                for u in range(RING):
                    for lead, step in stages:
                        step(i, u + lead)
            if turn:
                turn(SLOTS // RING - 1, RING)
            for u in range(RING):
                for lead, step in stages:
                    if u + lead < RING:
                        step(SLOTS // RING - 1, u + lead)

        @block.sync
        def _(sp):
            def load_x(g, it, h, last):
                sp.wait_ge(s_x[h], 32 * it)
                for b in range(BATCHES):
                    src = tokens[bass.ds(g * 2 * P + b * SEQ, 2 * P), :].rearrange("(k p) d -> p k d", p=P)
                    dst = x_all[:, bass.ds(g * GROUP_TILES, GROUP_TILES), :].rearrange(
                        "p (k b) d -> p b k d", b=BATCHES)[:, b]
                    sp.dma_start(dst, src).then_inc(s_x[h], 16)

            def load_x0(h):
                for b in range(BATCHES):
                    src = tokens[h * 2 * P + b * SEQ:(h + 1) * 2 * P + b * SEQ, :].rearrange("(k p) d -> p k d", p=P)
                    dst = x_all[:, h * GROUP_TILES:(h + 1) * GROUP_TILES, :].rearrange(
                        "p (k b) d -> p b k d", b=BATCHES)[:, b]
                    sp.dma_start(dst, src).then_inc(s_x[h], 16)

            sp.sem_inc(s_free, SPARE_FREE)
            load_x0(0)
            sp.dma_start(w_tok[:, :, :], w_tok_t.rearrange("(c p) n -> p c n", p=P)).then_inc(s_wtok, 16)
            sp.dma_start(nw[:, :], norm_w).then_inc(s_nw, 16)
            load_x0(1)
            for b in range(BATCHES):
                sp.dma_start(w_out[b][b * N:(b + 1) * N, :], w_out_t).then_inc(s_wout, 16)
            with sp.Fori(1, GROUPS // 2) as it:
                for h in range(2):
                    load_x(it * 2 + h, it, h, False)
            sp.dma_start(w_gu[:, :], w_gate_up_t.rearrange("p e n -> p (e n)")).then_inc(s_wgu, 16)
            sp.dma_start(w_dn[:, :], w_down_t.rearrange("p e n -> p (e n)")).then_inc(s_wdn, 16)
            sp.wait_ge(s_const, 2)
            sp.dma_start(table[PAD_BLOCK:PAD_BLOCK + P, :], pad_rows[:, :]).then_inc(s_padblk, 16)

            def rows_sent(g, it, h, left):
                if left == 2:
                    sp.wait_ge(s_sent[h], (it + 1) * 16 * GROUP_TILES)
                    sp.sem_inc(s_free, 1)

            over_groups(sp, rows_sent)

            def first_rows(i):
                regs = [sp.alloc_register(f"first_row{i if isinstance(i, int) else ''}_{u}") for u in range(RING)]
                sp.load(regs, first_row[0:1, bass.ds(i * RING, RING)])
                return [bass.RuntimeValue.of_register_unchecked(r, min_val=0, max_val=PAD_BLOCK) for r in regs]

            sp.wait_ge(s_tab, 1)
            for h in range(2):
                sp.wait_ge(s_sent[h], 16 * GROUP_TILES * (GROUPS // 2))
            sp.wait_ge(s_padblk, 16)

            def load_blocks(i, reused):
                for u, r in enumerate(first_rows(i)):
                    if reused:
                        sp.wait_ge(s_out[u], i * 16)
                    sp.dma_start(block_in[u][:, :], table[bass.ds(r, P), :]).then_inc(s_in[u], 16)

            load_blocks(0, False)
            for r in first_rows(SLOTS // RING):
                sp.dma_start(table[bass.ds(r, P), :], pad_rows[:, :]).then_inc(s_pad, 16)
            with sp.Fori(1, FULL_SLOTS // RING) as i:
                load_blocks(i, True)
            sp.wait_ge(s_pad, 16 * E)
            with sp.Fori(FULL_SLOTS // RING, SLOTS // RING) as i:
                load_blocks(i, True)
            for u in range(RING):
                sp.wait_ge(s_out[u], 16 * (SLOTS // RING))

        @block.gpsimd
        def _(pool):
            pool.memset(minus_half[:, :], -0.5).then_inc(s_set, 1)
            pool.memset(ident[:, :], 0.0).then_inc(s_set, 1)
            pool.memset(before[:, :], 1.0).then_inc(s_set, 1)
            pool.wait_ge(s_set, 3)
            pool.affine_select(out=ident[:, :], in_=ident[:, :], compare_op=ALU.not_equal, fill=1.0, base=0,
                               pattern=[[-1, P]], channel_multiplier=1).then_inc(s_set, 1)
            pool.affine_select(out=before[:, :], in_=before[:, :], compare_op=ALU.is_gt, fill=0.0, base=0,
                               pattern=[[1, P]], channel_multiplier=-1).then_inc(s_set, 1)
            pool.memset(ones[:, :], 1.0)
            pool.memset(ones_e[:, :], 1.0)
            pool.wait_ge(s_set, 5)
            pool.memset(state[1][:, P - 1:P], 0.0)
            pool.memset(restart[:, :, 1:], 1.0)
            pool.memset(restart[:, :, 0:1], 0.0)
            pool.memset(counted[:, :, GROUP_TILES:], 0.0)
            iota = dict(allow_small_or_imprecise_dtypes=True)
            pool.iota(rev[:, :], pattern=[[-1, E]], base=E, channel_multiplier=0, **iota)
            pool.iota(ebase[:, :], pattern=[[REGION, E]], base=0, channel_multiplier=0, **iota)
            pool.iota(token_ids[:, :], pattern=[[2 * P, GROUPS], [P, 2], [SEQ, BATCHES]], base=0,
                      channel_multiplier=1)
            for h in range(2):
                pool.memset(row[h][:, :, ID_COL + 1:ROW], 0.0)
            pool.iota(slot_no[:, :], pattern=[[1, FULL_SLOTS]], base=0, channel_multiplier=0, **iota)
            pool.iota(slot_row[:, :], pattern=[[P, FULL_SLOTS]], base=0, channel_multiplier=0, **iota)
            pool.iota(expert_of[:, FULL_SLOTS:SLOTS], pattern=[[1, E]], base=0, channel_multiplier=0).then_inc(s_const, 1)
            pool.memset(pad_rows[:, 0:ID_COL], 0.0)
            pool.memset(pad_rows[:, ID_COL:ROW].bitcast(I32), NO_TOKEN).then_inc(s_const, 1)

            def powers(g, h):
                pool.wait_ge(s_stats, g + 1)
                pool.tensor_tensor(pow_out[h][:, :, :], pow_in[h][:, :, :],
                                   minus_half[:, :].rearrange("p (a t) -> p a t", a=2), ALU.pow).then_inc(s_pow, 1)

            powers(0, 0)
            powers(1, 1)

            def group(g, it, h, left):
                if left == 2:
                    powers(g + 2, h)
                pool.wait_ge(s_place, g + 1)
                pool.wait_ge(s_xs, g + 1 + SPARE_XS)
                for t in range(GROUP_TILES):
                    pool.wait_ge(s_base, g * GROUP_TILES + t + 1 + SPARE_BASE)
                    pool.sem_inc(s_go, 1)
                    pool.indirect_dma_start(table, bass.IndirectOffsetOnAxis(place[h][:, t:t + 1], 0),
                                            row[h][:, t, :], None).then_inc(s_sent[h], 16)

            over_groups(pool, group)

            def send(i, u):
                pool.wait_ge(s_r, i * RING + u + 1 + SPARE_RING)
                pool.sem_inc(s_go, 1)
                pool.indirect_dma_start(
                    out, bass.IndirectOffsetOnAxis(block_in[u][:, ID_COL:ID_COL + 1].bitcast(I32), 0),
                    result[u][:, :], None, bounds_check=TOKENS - 1, oob_is_err=False).then_inc(s_out[u], 16)

            with pool.Fori(0, SLOTS // RING) as i:
                for u in range(RING):
                    send(i, u)

        @block.scalar
        def _(a):
            a.dma_start(decay[0:N, :], log_decay.rearrange("(n o) -> n o", o=1)).then_inc(s_decay, 16)
            a.dma_start(decay[N:2 * N, :], log_decay.rearrange("(n o) -> n o", o=1)).then_inc(s_decay, 16)
            one_row = lambda v: v.rearrange("(o n) -> o n", o=1)
            a.wait_ge(s_bias0, 1)
            for r in (0, P // 2):
                a.dma_start(bias_in[r:r + 1, 0:D], one_row(b_out)).then_inc(s_bias, 16)
                a.dma_start(bias_in[r + 1:r + 2, 0:D], one_row(b_skip)).then_inc(s_bias, 16)
                a.dma_start(bias_in[r:r + 1, D + E:PROJ], one_row(b_in)).then_inc(s_bias, 16)
            a.wait_ge(s_const, 1)
            a.activation(func_set[:, :], minus_half[:, 0:1], ACT.Silu)
            a.wait_ge(s_decay, 32)
            a.activation(decay[:, :], decay[:, :], ACT.Tanh, scale=0.5).then_inc(s_aset, 1)
            a.wait_ge(s_bias, 16 * 6)
            a.activation(bias[:, :], bias_in[:, :], ACT.Copy).then_inc(s_aset, 1)

            a.sem_inc(s_xT, SPARE_XT)
            a.sem_inc(s_xs, SPARE_XS)
            a.sem_inc(s_bT, SPARE_RING)
            a.sem_inc(s_aT, SPARE_RING)

            def copy_xT(s, k):
                a.wait_ge(s_psxT, s + 1)
                a.wait_ge(s_y, (s - 1) * BATCHES + SPARE_Y)
                a.activation(xT[k][:, :, :, :].rearrange("p c b n -> p (c b n)"), ps_xT[k][:, :],
                             ACT.Copy).then_inc(s_xT, 1)

            def copy_lu(s, h, k):
                a.wait_ge(s_y, (s + 1) * BATCHES + SPARE_Y)
                tiles = slice(BATCHES * k, BATCHES * (k + 1))
                y = banks[:, 2 + 2 * k:4 + 2 * k, :]
                a.activation(logits[h][:, tiles, :], y[:, :, D:D + E], ACT.Copy)
                a.activation(inputs[h][:, tiles, :], y[:, :, D + E:PROJ], ACT.Copy).then_inc(s_lu, 1)

            def residual(g, h, k):
                if k == 0:
                    a.wait_ge(s_coef, g + 1)
                for t in range(k * BATCHES, (k + 1) * BATCHES):
                    ins = a.activation(res[h][:, t, :], x_all[:, bass.ds(g * GROUP_TILES + t, 1), :].rearrange(
                        "p o d -> p (o d)"), ACT.Identity, bias=res_bias[h][:, t:t + 1],
                        scale=res_scale[h][:, t:t + 1])
                ins.then_inc(s_res, 1)

            copy_xT(0, 0)
            copy_xT(1, 1)
            copy_lu(0, 0, 0)

            def group(g, it, h, left):
                residual(g, h, 0)
                copy_lu(g * 2 + 1, h, 1)
                if left:
                    copy_xT(g * 2 + 2, 0)
                residual(g, h, 1)
                a.wait_ge(s_top, g + 1)
                a.activation(tanh_top[:, :], top_true[:, :], ACT.Tanh, scale=0.5).then_inc(s_tanh, 1)
                if left:
                    copy_lu(g * 2 + 2, 1 - h, 0)
                    copy_xT(g * 2 + 3, 1)
                a.wait_ge(s_xss, g + 1)
                a.wait_ge(s_free, g - 1 + SPARE_FREE)
                for t in range(GROUP_TILES):
                    ins = a.activation(row[h][:, t, 0:D], xr[h][:, t, :], ACT.Copy, scale=xs_scale[:, t:t + 1])
                ins.then_inc(s_xs, 1)

            over_groups(a, group)

            def copy_bT(i, u):
                a.wait_ge(s_psbT, i * RING + u + 1)
                a.wait_ge(s_gu, i * RING + u - 1 + SPARE_RING)
                a.activation(bT[u % 2][:, :], ps_bT[u % 2][:, 0:DC * P], ACT.Copy).then_inc(s_bT, 1)

            def gate(i, u):
                a.wait_ge(s_gu, i * RING + u + 1 + SPARE_RING)
                a.wait_ge(s_act, i * RING + u - 1 + SPARE_RING)
                a.activation(silu[u % 2][:, :], ps_gu[u % 2][:, 0:INNER], ACT.Silu).then_inc(s_silu, 1)

            def copy_aT(i, u):
                a.wait_ge(s_psaT, i * RING + u + 1)
                a.wait_ge(s_dn, i * RING + u - 1 + SPARE_RING)
                a.activation(aT[u % 2][:, :], ps_aT[u % 2][:, 0:P], ACT.Copy).then_inc(s_aT, 1)

            over_blocks(a, [(3, copy_bT), (2, gate), (1, copy_aT)])

        @block.tensor
        def _(pe):
            pe.sem_inc(s_y, SPARE_Y)
            pe.sem_inc(s_gu, SPARE_RING)
            pe.sem_inc(s_dn, SPARE_RING)

            def transpose_x(s, h, k):
                pe.wait_ge(s_xr, s + 1)
                pe.wait_ge(s_xT, s - 1 + SPARE_XT)
                for c in range(DC):
                    for b in range(BATCHES):
                        ins = pe.transpose(ps_xT[k][:, (c * BATCHES + b) * P:(c * BATCHES + b + 1) * P],
                                           xr[h][:, 2 * k + b, c * P:(c + 1) * P], ident[:, :])
                ins.then_inc(s_psxT, 1)

            def project(s, k):
                pe.wait_ge(s_xT, s + 1 + SPARE_XT)
                for b in range(BATCHES):
                    pe.wait_ge(s_base, (s - 2) * BATCHES + b + 1 + SPARE_BASE)
                    y = ps_y[2 * k + b][:, 0:PROJ]
                    pe.matmul(y, ones_r[:, :], bias[:, :], start=True, stop=False)
                    for c in range(DC):
                        ins = pe.matmul(y, xT[k][:, c, b, :], w_tok[:, c, :], start=False, stop=(c == DC - 1))
                    ins.then_inc(s_y, 1)

            def transpose_u(s, h, k):
                pe.wait_ge(s_lu, s + 1)
                pe.wait_ge(s_scan, s + SPARE_SCAN)
                pe.transpose(ps_uT[:, 0:P], inputs[h][:, 2 * k:2 * k + 2, :].rearrange("p b n -> p (b n)"), ident[:, :]).then_inc(s_uT, 1)

            def project_states(s, k):
                pe.wait_ge(s_scan, s + 1 + SPARE_SCAN)
                for b in range(BATCHES):
                    pe.matmul(ps_y[2 * k + b][:, 0:D], state[k][:, :], w_out[b][:, :], start=False, stop=True,
                              skip_group_check=True).then_inc(s_wo, 1)

            pe.wait_ge(s_const, 1)
            transpose_x(0, 0, 0)
            transpose_x(1, 0, 1)
            pe.wait_ge(s_wready, 1)
            pe.wait_ge(s_wout, 16 * BATCHES)
            project(0, 0)

            def group(g, it, h, left):
                transpose_u(g * 2, h, 0)
                project(g * 2 + 1, 1)
                if left:
                    transpose_x(g * 2 + 2, 1 - h, 0)
                project_states(g * 2, 0)
                transpose_u(g * 2 + 1, h, 1)
                if left:
                    project(g * 2 + 2, 0)
                    transpose_x(g * 2 + 3, 1 - h, 1)
                pe.wait_ge(s_ch, g + 1)
                ranks = ps_rank[:, 0:E * GROUP_TILES].rearrange("p (e t) -> p e t", e=E)
                pe.matmul(ranks, before[:, :], chosen[:, :, 1:], start=True, stop=False)
                pe.matmul(ranks, ones[:, :], counted[:, :, 0:GROUP_TILES], start=False, stop=True).then_inc(s_rank, 1)
                project_states(g * 2 + 1, 1)

            over_groups(pe, group)
            pe.wait_ge(s_place, GROUPS)
            pe.matmul(ps_rank[:, 0:E], ones[:, :], counted[:, :, GROUP_TILES], start=True, stop=True).then_inc(s_cnt, 1)

            pe.wait_ge(s_tab, 1)
            pe.wait_ge(s_wgu, 16)
            pe.wait_ge(s_wdn, 16)

            experts = []

            def load_experts(i, n):
                regs = [pe.alloc_register(f"experts{n}_{u}") for u in range(n)]
                pe.load(regs, expert_of[0:1, bass.ds(i * RING, n)])
                experts[:] = [bass.RuntimeValue.of_register_unchecked(r, min_val=0, max_val=E - 1) for r in regs]

            def transpose_block(i, u):
                pe.wait_ge(s_in[u % RING], i * 16 + (u // RING + 1) * 16)
                pe.wait_ge(s_bT, i * RING + u - 1 + SPARE_RING)
                for c in range(DC):
                    ins = pe.transpose(ps_bT[u % 2][:, c * P:(c + 1) * P], block_in[u % RING][:, c * P:(c + 1) * P],
                                       ident[:, :])
                ins.then_inc(s_psbT, 1)

            def gate_up(i, u):
                pe.wait_ge(s_bT, i * RING + u + 1 + SPARE_RING)
                pe.wait_ge(s_act, i * RING + u - 1 + SPARE_RING)
                for c in range(DC):
                    ins = pe.matmul(ps_gu[u % 2][:, 0:2 * INNER], bT[u % 2][:, c * P:(c + 1) * P],
                                    w_gu[:, bass.ds(experts[u] * (DC * 2 * INNER) + c * 2 * INNER, 2 * INNER)],
                                    start=(c == 0), stop=(c == DC - 1))
                ins.then_inc(s_gu, 1)

            def transpose_act(i, u):
                pe.wait_ge(s_act, i * RING + u + 1 + SPARE_RING)
                pe.wait_ge(s_aT, i * RING + u - 1 + SPARE_RING)
                pe.transpose(ps_aT[u % 2][:, 0:P], act[u % 2][:, :], ident[:, :]).then_inc(s_psaT, 1)

            def down(i, u):
                pe.wait_ge(s_aT, i * RING + u + 1 + SPARE_RING)
                pe.wait_ge(s_r, i * RING + u - 1 + SPARE_RING)
                pe.matmul(ps_dn[u % 2][:, 0:D], aT[u % 2][:, :], w_dn[:, bass.ds(experts[u] * D, D)],
                          start=True, stop=True).then_inc(s_dn, 1)

            over_blocks(pe, [(3, transpose_block), (2, gate_up), (1, transpose_act), (0, down)], load_experts)

        @block.vector
        def _(v):
            v.sem_inc(s_scan, SPARE_SCAN)
            v.sem_inc(s_base, SPARE_BASE)
            v.sem_inc(s_act, SPARE_RING)
            v.sem_inc(s_r, SPARE_RING)
            step = Step(v, s_v)

            def statistics(g, it, h, part=None):
                if part != 1:
                    v.wait_ge(s_x[h], it * 32 + 32)
                for t in range(2 if part == 1 else 0, 2 if part == 0 else GROUP_TILES):
                    ins = v.bn_stats(stats[h][:, t, :], x_all[:, bass.ds(g * GROUP_TILES + t, 1), :].rearrange(
                        "p o d -> p (o d)"))
                if part == 0:
                    return
                step(ins)
                v.memset(nothing[:, :], 0.0)
                for t in range(GROUP_TILES):
                    ins = v.bn_aggr(mean_var[h][:, t, :], stats[h][:, t, :])
                step(ins)
                v.tensor_scalar(pow_in[h][:, 0, :], mean_var[h][:, :, 1], 1.0 + RMS_EPS, LN_EPS * RMS_EPS,
                                ALU.mult, ALU.add)
                v.tensor_scalar(pow_in[h][:, 1, :], mean_var[h][:, :, 1], LN_EPS, None, ALU.add).then_inc(s_stats, 1)

            def normalise(g, h):
                v.wait_ge(s_pow, g + 1)
                v.wait_ge(s_xs, g - 1 + SPARE_XS)
                for t in range(GROUP_TILES):
                    ins = v.tensor_scalar(xr[h][:, t, :], x_all[:, bass.ds(g * GROUP_TILES + t, 1), :].rearrange(
                        "p o d -> p (o d)"), mean_var[h][:, t, 0:1], pow_out[h][:, 0, t:t + 1],
                        ALU.subtract, ALU.mult)
                    if t % 2:
                        ins.then_inc(s_xr, 1)
                v.tensor_scalar(res_scale[h][:, :], pow_out[h][:, 1, :], 1.0, None, ALU.add)
                v.scalar_tensor_tensor(res_bias[h][:, :], mean_var[h][:, :, 0], -1.0, pow_out[h][:, 1, :],
                                       ALU.mult, ALU.mult).then_inc(s_coef, 1)
                step(v.tensor_tensor(inv_rms[h][:, :], pow_out[h][:, 0, :], pow_out[h][:, 1, :], ALU.mult))
                step(v.tensor_tensor(inv_rms[h][:, :], inv_rms[h][:, :], pow_in[h][:, 0, :], ALU.mult))

            def scan(s, k):
                v.wait_ge(s_uT, s + 1)
                v.tensor_tensor_scan(state[k][:, :], decay[:, 0:1].to_broadcast([P, P]), ps_uT[:, 0:P],
                                     state[1 - k][:, P - 1:P], ALU.mult, ALU.add).then_inc(s_scan, 1)

            def add_residual(g, it, h, k):
                v.wait_ge(s_res, g * 2 + k + 1)
                if k == 0:
                    v.wait_ge(s_free, g - 1 + SPARE_FREE)
                    v.tensor_copy(row[h][:, :, ID_COL].bitcast(I32),
                                  token_ids[:, bass.ds(g * GROUP_TILES, GROUP_TILES)])
                for b in range(BATCHES):
                    v.wait_ge(s_wo, (g * 2 + k) * BATCHES + b + 1)
                    v.tensor_tensor(row[h][:, 2 * k + b, D:2 * D], ps_y[2 * k + b][:, 0:D], res[h][:, 2 * k + b, :],
                                    ALU.add).then_inc(s_base, 1)

            def choose(g, h):
                by_tile = [P, GROUP_TILES, E]
                step(v.tensor_reduce(top[:, :], logits[h][:, :, :], AX, ALU.max))
                v.tensor_tensor(top_true[:, :], top[:, :], inv_rms[h][:, :], ALU.mult).then_inc(s_top, 1)
                step(v.tensor_tensor(is_top[:, :, :], logits[h][:, :, :], top[:, :].unsqueeze(2).to_broadcast(by_tile), ALU.is_ge))
                step(v.tensor_tensor(cand[:, :, :], is_top[:, :, :], rev[:, :].unsqueeze(1).to_broadcast(by_tile),
                                     ALU.mult))
                step(v.tensor_reduce(first[:, :], cand[:, :, :], AX, ALU.max))
                v.tensor_copy(chosen[:, :, 0:1], counted[:, :, GROUP_TILES:])
                step(v.tensor_tensor(chosen[:, :, 1:].rearrange("p e t -> p t e"),
                                     rev[:, :].unsqueeze(1).to_broadcast(by_tile),
                                     first[:, :].unsqueeze(2).to_broadcast(by_tile), ALU.is_equal))
                v.tensor_tensor_scan(counted[:, :, :].rearrange("p e t -> p (e t)"),
                                     restart[:, :, :].rearrange("p e t -> p (e t)"),
                                     chosen[:, :, :].rearrange("p e t -> p (e t)"), 0.0,
                                     ALU.mult, ALU.add).then_inc(s_ch, 1)

            def scale_of_rows(g, h):
                v.wait_ge(s_tanh, g + 1)
                step(v.tensor_scalar(weight[:, :], tanh_top[:, :], 0.5, 0.5, ALU.mult, ALU.add))
                v.tensor_tensor(xs_scale[:, :], weight[:, :], inv_rms[h][:, :], ALU.mult).then_inc(s_xss, 1)

            def places(g, h):
                v.wait_ge(s_rank, g + 1)
                step(v.tensor_tensor(at_all[:, :, :], ps_rank[:, 0:E * GROUP_TILES].rearrange("p (e t) -> p e t", e=E),
                                     ebase[:, :].unsqueeze(2).to_broadcast([P, E, GROUP_TILES]), ALU.add))
                step(v.tensor_tensor(at_own[:, :, :], at_all[:, :, :], chosen[:, :, 1:], ALU.mult))
                step(v.tensor_reduce(place_f[:, :], at_own[:, :, :].rearrange("p e t -> p t e"), AX, ALU.add))
                v.tensor_copy(place[h][:, :], place_f[:, :]).then_inc(s_place, 1)

            v.memset(bias_in[:, :], 0.0).then_inc(s_bias0, 1)
            for b in range(BATCHES):
                v.memset(w_out[b][(1 - b) * N:(2 - b) * N, :], 0.0)
            v.memset(ones_r[:, :].bitcast(F32), 1.0)
            statistics(0, 0, 0)
            v.wait_ge(s_wtok, 16)
            v.wait_ge(s_nw, 16)
            for c in range(DC):
                for lo, hi in ((0, D), (D + E, PROJ)):
                    v.tensor_scalar(w_tok[:, c, lo:hi], w_tok[:, c, lo:hi], nw[:, c:c + 1], None, ALU.mult)
            v.wait_ge(s_aset, 2)
            v.tensor_scalar(decay[:, :], decay[:, :], 0.5, 0.5, ALU.mult, ALU.add)
            v.tensor_tensor(bias[P // 2:P, :], bias_in[P // 2:P, :], bias[P // 2:P, :].bitcast(F32),
                            ALU.subtract).then_inc(s_wready, 1)
            v.wait_ge(s_const, 1)
            normalise(0, 0)
            statistics(1, 0, 1)
            before_groups = step.n

            def group(g, it, h, left):
                step.begin(g * STEP_COUNT + before_groups)
                scan(g * 2, 0)
                if left:
                    normalise(g + 1, 1 - h)
                if left == 2:
                    statistics(g + 2, it + 1, h, 0)
                add_residual(g, it, h, 0)
                scan(g * 2 + 1, 1)
                choose(g, h)
                scale_of_rows(g, h)
                if left == 2:
                    statistics(g + 2, it + 1, h, 1)
                if left:
                    add_residual(g, it, h, 1)
                    places(g, h)
                else:
                    places(g, h)
                    add_residual(g, it, h, 1)
                assert left < 2 or step.n == STEP_COUNT, step.n
                step.skip(STEP_COUNT)

            over_groups(v, group)
            step.begin(GROUPS * STEP_COUNT + before_groups)

            v.wait_ge(s_cnt, 1)
            step(v.tensor_copy(count[:, :], ps_rank[:, 0:E]))
            v.tensor_tensor(first_row[:, PADS:PADS + E], count[:, :], ebase[:, :], ALU.add)
            step(v.tensor_copy(count_i[:, :], count[:, :]))
            step(v.tensor_scalar(full_i[:, :], count_i[:, :], 7, None, ALU.arith_shift_right))
            step(v.tensor_copy(full[:, :], full_i[:, :]))
            v.scalar_tensor_tensor(first_row[:, FULL_SLOTS:SLOTS], full[:, :], float(P), ebase[:, :], ALU.mult, ALU.add)
            step(v.tensor_tensor_scan(full_end[:, :], ones_e[:, :], full[:, :], 0.0, ALU.mult, ALU.add))
            by_slot = [P, FULL_SLOTS, E]
            step(v.tensor_tensor(done_e[:, :, :], slot_no[:, :].unsqueeze(2).to_broadcast(by_slot),
                                 full_end[:, :].unsqueeze(1).to_broadcast(by_slot), ALU.is_ge))
            v.tensor_reduce(slot_e[:, :], done_e[:, :, :], AX, ALU.add)
            step(v.tensor_tensor(done_f[:, :, :], done_e[:, :, :], full[:, :].unsqueeze(1).to_broadcast(by_slot),
                                 ALU.mult))
            v.scalar_tensor_tensor(slot_a[:, :], slot_e[:, :], float(REGION), slot_row[:, :], ALU.mult, ALU.add)
            step(v.tensor_reduce(slot_f[:, :], done_f[:, :, :], AX, ALU.add))
            v.tensor_scalar(expert_of[:, 0:FULL_SLOTS], slot_e[:, :], float(E - 1), None, ALU.min)
            step(v.scalar_tensor_tensor(slot_b[:, :], slot_f[:, :], -float(P), slot_a[:, :], ALU.mult, ALU.add))
            v.tensor_scalar(first_row[:, 0:FULL_SLOTS], slot_b[:, :], float(PAD_BLOCK), None,
                            ALU.min).then_inc(s_tab, 1)

            def product(i, u):
                v.wait_ge(s_silu, i * RING + u + 1)
                v.tensor_tensor(act[u % 2][:, :], ps_gu[u % 2][:, INNER:2 * INNER], silu[u % 2][:, :],
                                ALU.mult).then_inc(s_act, 1)

            def add_terms(i, u):
                v.wait_ge(s_dn, i * RING + u + 1 + SPARE_RING)
                v.tensor_tensor(result[u % RING][:, :], ps_dn[u % 2][:, 0:D], block_in[u % RING][:, D:2 * D],
                                ALU.add).then_inc(s_r, 1)

            over_blocks(v, [(2, product), (0, add_terms)])


class Step:

    def __init__(self, eng, sem):
        self.eng, self.sem, self.base, self.n = eng, sem, 0, 0

    def begin(self, base):
        self.base, self.n = base, 0

    def __call__(self, ins):
        ins.then_inc(self.sem, 1)
        self.n += 1
        self.eng.wait_ge(self.sem, self.base + self.n)

    def skip(self, n):
        if self.n < n:
            self.eng.sem_inc(self.sem, n - self.n)


def kernel(L0_attn_tokens, L0_attn_norm_w, L0_attn_W_in, L0_attn_b_in, L0_attn_W_out, L0_attn_b_out,
           L0_attn_W_skip, L0_attn_b_skip, L0_attn_log_decay, L0_ffn_gate_w, L0_ffn_w_gate, L0_ffn_w_up,
           L0_ffn_w_down):
    import concourse.bacc as bacc
    from concourse.bass_utils import run_bass_kernel_spmd

    B, S, D = L0_attn_tokens.shape
    E, I, _ = L0_ffn_w_gate.shape
    w_tok = np.concatenate([np.asarray(w).T for w in (L0_attn_W_skip, L0_ffn_gate_w, L0_attn_W_in)], axis=1)
    w_gu = np.stack([np.asarray(L0_ffn_w_gate), np.asarray(L0_ffn_w_up)], axis=1)
    w_gu = w_gu.reshape(E, 2, I, D // P, P).transpose(4, 0, 3, 1, 2).reshape(P, E, -1)
    arrays = {
        "tokens": np.asarray(L0_attn_tokens).reshape(B * S, D),
        "w_tok_t": w_tok,
        "norm_w": np.asarray(L0_attn_norm_w).reshape(D // P, P).T,
        "w_out_t": np.asarray(L0_attn_W_out).T,
        "b_in": L0_attn_b_in,
        "b_out": L0_attn_b_out,
        "b_skip": L0_attn_b_skip,
        "log_decay": L0_attn_log_decay,
        "w_gate_up_t": w_gu,
        "w_down_t": np.asarray(L0_ffn_w_down).transpose(2, 0, 1),
    }
    arrays = {name: np.ascontiguousarray(a) for name, a in arrays.items()}
    nc = bacc.Bacc("TRN2", target_bir_lowering=False, num_devices=1)
    args = {name: nc.dram_tensor(name, a.shape, F32, kind="ExternalInput").ap() for name, a in arrays.items()}
    out = nc.dram_tensor("out", (B * S, D), F32, kind="ExternalOutput").ap()
    program(nc, **args, out=out)
    r = run_bass_kernel_spmd(nc, [arrays], core_ids=[0])
    return r.results[0]["out"].reshape(B, S, D)
```
